# Optimizing a Trainium2 kernel written in Bass

```python
import numpy as np
import jax
import jax.numpy as jnp

def _softmax(x, axis=-1):
    return jax.nn.softmax(x, axis=axis)

def _gelu(x):
    return jax.nn.gelu(x, approximate=True)

def _silu(x):
    return jax.nn.silu(x)

def _sigmoid(x):
    return jax.nn.sigmoid(x)

def _layernorm(x, axis=-1, eps=1e-05):
    m = jnp.mean(x, axis=axis, keepdims=True)
    v = jnp.var(x, axis=axis, keepdims=True)
    return (x - m) / jnp.sqrt(v + eps)

def _scatter_add(tgt, idx, src, axis=0):
    return tgt.at[idx].add(src)

def _segment_sum(src, seg, n):
    return jax.ops.segment_sum(src, seg, n)
kernel_name = 'mk_adaln_ffn_d1_seqx_r8_a91e5d'

def setup_inputs(seed: int=0):
    np.random.seed(seed)
    _w = jnp.asarray

    def _rec_inputs():
        import jax
        import jax.numpy as jnp
        _rk = jax.random.key(seed)
        x = -7.109e-05 + 0.9999 * jax.random.normal(jax.random.fold_in(_rk, 1), (8, 128, 512), jnp.float32)
        _lenS = 128 - jax.random.randint(jax.random.fold_in(_rk, 7), (8,), 0, max(1, 128 // 4) + 1, jnp.int32)
        _lenS2 = 128 - jax.random.randint(jax.random.fold_in(_rk, 8), (8,), 0, max(1, 128 // 4) + 1, jnp.int32)
        itok_B_1_14 = jax.random.randint(jax.random.fold_in(_rk, 11), (8,), 1, 15, jnp.int32)
        return (x, itok_B_1_14)
    x, itok_B_1_14 = _rec_inputs()

    def _L0_cond_setup():
        import jax, jax.numpy as jnp
        import numpy as np
        B, S, D_IN = (8, 256, 512)
        A, D_OUT = (16, 512)
        key = jax.random.key(seed)
        k1, k2, k3 = jax.random.split(key, 3)
        x = jax.random.normal(k1, (B, S, D_IN), dtype=jnp.float32)
        weight = jax.random.normal(k2, (A, D_OUT, D_IN), dtype=jnp.float32) * 0.02
        adapter_ids = jax.random.randint(k3, (B,), 0, A, dtype=jnp.int64)
        return {'x': x, 'weight': weight, 'adapter_ids': adapter_ids}
    _L0_cond_all = _L0_cond_setup()
    _L0_cond_in = {k: v for k, v in _L0_cond_all.items() if k in ('weight',)}
    del _L0_cond_all

    def _L0_ffn_setup():
        import jax, jax.numpy as jnp
        import numpy as np
        IMAGE_START_POS = 34
        Q_START = IMAGE_START_POS + 72 + 1
        Q_END = -1
        LORA_ALPHA = 32
        LORA_RANK = 16
        SCALING = LORA_ALPHA / LORA_RANK
        key = jax.random.key(seed)
        ks = jax.random.split(key, 7)
        B_, S, D, O, E, R = (4, 256, 512, 512, 8, LORA_RANK)
        s = 0.02
        return {'x': jax.random.normal(ks[0], (B_, S, D), jnp.float32), 'W': jax.random.normal(ks[1], (O, D), jnp.float32) * s, 'b': jax.random.normal(ks[2], (O,), jnp.float32) * s, 'A': jax.random.normal(ks[3], (E, R, D), jnp.float32) * s, 'B': jax.random.normal(ks[4], (E, O, R), jnp.float32) * s, 'router_W': jax.random.normal(ks[5], (E, D), jnp.float32) * s, 'router_b': jax.random.normal(ks[6], (E,), jnp.float32) * s}
    _L0_ffn_all = _L0_ffn_setup()
    _L0_ffn_in = {k: v for k, v in _L0_ffn_all.items() if k in ('W', 'b', 'A', 'B', 'router_W', 'router_b')}
    del _L0_ffn_all
    return {'x': x, 'itok_B_1_14': itok_B_1_14, 'L0_cond_weight': _L0_cond_in['weight'], 'L0_ffn_W': _L0_ffn_in['W'], 'L0_ffn_b': _L0_ffn_in['b'], 'L0_ffn_A': _L0_ffn_in['A'], 'L0_ffn_B': _L0_ffn_in['B'], 'L0_ffn_router_W': _L0_ffn_in['router_W'], 'L0_ffn_router_b': _L0_ffn_in['router_b']}

def reference(x, itok_B_1_14, L0_cond_weight, L0_ffn_W, L0_ffn_b, L0_ffn_A, L0_ffn_B, L0_ffn_router_W, L0_ffn_router_b):
    import jax
    import jax.numpy as jnp

    def _L0_cond_ref(x, weight, adapter_ids):
        import jax, jax.numpy as jnp
        import numpy as np
        B, S, D_IN = (8, 256, 512)
        A, D_OUT = (16, 512)
        w = weight[adapter_ids]
        return jnp.einsum('bij,bkj->bik', x, w)

    def _L0_ffn_ref(x, W, b, A, B, router_W, router_b):
        import jax, jax.numpy as jnp
        import numpy as np
        IMAGE_START_POS = 34
        Q_START = IMAGE_START_POS + 72 + 1
        Q_END = -1
        LORA_ALPHA = 32
        LORA_RANK = 16
        SCALING = LORA_ALPHA / LORA_RANK
        x_q = x[:, Q_START:Q_END, :]
        q = x_q.mean(axis=1)
        logits = q @ router_W.T + router_b
        routing = jax.nn.softmax(logits, axis=-1)
        base = x @ W.T + b
        t = jnp.einsum('bsd,erd->bser', x, A)
        lora = jnp.einsum('bser,eor,be->bso', t, B, routing) * SCALING
        return base + lora
    x = x + _L0_ffn_ref(_L0_cond_ref(x, L0_cond_weight, itok_B_1_14), L0_ffn_W, L0_ffn_b, L0_ffn_A, L0_ffn_B, L0_ffn_router_W, L0_ffn_router_b)
    return x

_drawn_inputs = setup_inputs


def setup_inputs(seed=0):
    import zlib

    import numpy as np

    out = dict(_drawn_inputs(seed))
    spreads = {}
    factors = {'L0_ffn_b': 2.909,
     'L0_ffn_A': 4.662,
     'L0_ffn_B': 4.658,
     'L0_ffn_router_W': 8.0,
     'L0_ffn_router_b': 8.0}
    for name, (base, spread) in spreads.items():
        noise = np.random.default_rng([zlib.crc32(name.encode()), seed]).standard_normal(out[name].shape)
        drawn = base * np.exp(spread * noise) if base else spread * noise
        out[name] = jnp.asarray(drawn.astype(out[name].dtype))
    for name, factor in factors.items():
        out[name] = (out[name] * factor).astype(out[name].dtype)
    return out
```

```python
from contextlib import ExitStack

import concourse.bass as bass
from concourse import mybir

P = 128
F32 = mybir.dt.float32
F32R = mybir.dt.float32r
ALU = mybir.AluOpType
ACT = mybir.ActivationFunctionType

Q_START, Q_END = 107, 127
LORA_SCALE = 2.0
F32_MAX = 3.4028235e38


def adapter_lora_kernel(nc, x, xT, ids, wcT, wT, azT, bT, bias, rbias, out):
    B, S, D = x.shape
    C = D // P
    NADAPT = wcT.shape[0]
    E = rbias.shape[1]
    ER = bT.shape[0]
    R = ER // E
    TZ = ER + E
    assert S == P and ER == P and C == 4 and B % 2 == 0

    with ExitStack() as ctx:
        def sb(name, shape, dt=F32):
            return ctx.enter_context(nc.sbuf_tensor(name, shape, dt))

        def psum(name):
            return ctx.enter_context(nc.psum_tensor(name, [P, D], F32))

        def sem(name):
            return ctx.enter_context(nc.semaphore(name))

        xT_raw = [sb(f"xT_raw{p}", [P, C, S]) for p in range(2)]
        wc_raw = [sb(f"wc_raw{p}", [P, C, D]) for p in range(2)]
        x_nat = [sb(f"x_nat{p}", [P, D]) for p in range(2)]
        xb = [sb(f"xb{p}", [P, D]) for p in range(2)]
        xT_hi = [sb(f"xT_hi{p}", [P, C, S], F32R) for p in range(2)]
        xT_lo = [sb(f"xT_lo{p}", [P, C, S], F32R) for p in range(2)]
        wc_hi = [sb(f"wc_hi{p}", [P, C, D], F32R) for p in range(2)]
        wc_lo = [sb(f"wc_lo{p}", [P, C, D], F32R) for p in range(2)]
        w_raw = sb("w_raw", [P, C, D])
        w_hi = sb("w_hi", [P, C, D], F32R)
        w_lo = sb("w_lo", [P, C, D], F32R)
        az_raw = sb("az_raw", [P, C, TZ])
        az_hi = sb("az_hi", [P, C, TZ], F32R)
        az_lo = sb("az_lo", [P, C, TZ], F32R)
        b_raw = sb("b_raw", [P, D])
        b2 = sb("b2", [P, D])
        b_hi = sb("b_hi", [P, D], F32R)
        b_lo = sb("b_lo", [P, D], F32R)
        bias_bc = sb("bias_bc", [P, D])
        rbias_bc = sb("rbias_bc", [P, E])
        ident = sb("ident", [P, P])
        mean_w = sb("mean_w", [P, P])
        y_sb = sb("y_sb", [P, D])
        yT_hi = sb("yT_hi", [P, C, S], F32R)
        yT_lo = sb("yT_lo", [P, C, S], F32R)
        z_sb = sb("z_sb", [P, E])
        nlogit = sb("nlogit", [P, E])
        nmax = sb("nmax", [P, 1])
        expd = sb("expd", [P, E])
        esum = sb("esum", [P, 1])
        rsum = sb("rsum", [P, 1])
        ts = sb("ts", [P, ER])
        tsT_hi = sb("tsT_hi", [P, S], F32R)
        tsT_lo = sb("tsT_lo", [P, S], F32R)
        o_sb = [sb(f"o_sb{p}", [P, D]) for p in range(2)]

        ps_y = psum("ps_y")
        ps_yT = psum("ps_yT")
        ps_tz = psum("ps_tz")
        ps_logit = psum("ps_logit")
        ps_tsT = psum("ps_tsT")
        ps_o = [psum(f"ps_o{p}") for p in range(2)]

        xT_in = [sem(f"xT_in{p}") for p in range(2)]
        wc_in = [sem(f"wc_in{p}") for p in range(2)]
        wc0_in = [sem(f"wc0_in{c}") for c in range(C)]
        x_in = [sem(f"x_in{p}") for p in range(2)]
        w_in = sem("w_in")
        az_in = sem("az_in")
        b_in = sem("b_in")
        bias_in = sem("bias_in")
        rbias_in = sem("rbias_in")
        stored = [sem(f"stored{p}") for p in range(2)]
        ident_zeroed = sem("ident_zeroed")
        ident_ready = sem("ident_ready")
        mean_set = sem("mean_set")
        mean_ready = sem("mean_ready")
        w_hi_ready = sem("w_hi_ready")
        w_lo_ready = sem("w_lo_ready")
        az_hi_ready = sem("az_hi_ready")
        az_lo_ready = sem("az_lo_ready")
        b2_ready = sem("b2_ready")
        b_hi_ready = sem("b_hi_ready")
        b_lo_ready = sem("b_lo_ready")
        y_done = sem("y_done")
        yT_done = sem("yT_done")
        tz_done = sem("tz_done")
        logit_done = sem("logit_done")
        tsT_done = sem("tsT_done")
        o_done = sem("o_done")
        xb_ready = sem("xb_ready")
        y_copied = sem("y_copied")
        yT_hi_ready = sem("yT_hi_ready")
        yT_lo_ready = sem("yT_lo_ready")
        z_copied = sem("z_copied")
        nmax_ready = sem("nmax_ready")
        exp_ready = sem("exp_ready")
        rsum_ready = sem("rsum_ready")
        ts_ready = sem("ts_ready")
        tsT_hi_ready = sem("tsT_hi_ready")
        tsT_lo_ready = sem("tsT_lo_ready")
        o_ready = sem("o_ready")
        raw_chunk_done = sem("raw_chunk_done")
        xT_hi_ready = sem("xT_hi_ready")
        xT_lo_ready = sem("xT_lo_ready")
        wc_hi_ready = sem("wc_hi_ready")
        wc_lo_ready = sem("wc_lo_ready")

        PAIRS = B // 2
        SPLIT0 = 2
        NS = C - 1

        def flat(t):
            return t[:].rearrange("p c s -> p (c s)")

        block = ctx.enter_context(nc.Block())

        @block.sync
        def _(sp):
            def load_xT(b, slot):
                sp.dma_start(xT_raw[slot][:], xT[bass.ds(b, 1)].rearrange("b p c s -> (b p) c s"))\
                    .then_inc(xT_in[slot], 16)

            def load_wc(b, slot):
                a = sp.value_load(ids[0:1, bass.ds(b, 1)], min_val=0, max_val=NADAPT - 1)
                sp.dma_start(wc_raw[slot][:], wcT[bass.ds(a, 1)].rearrange("a p c o -> (a p) c o"))\
                    .then_inc(wc_in[slot], 16)

            def load_x(b, slot):
                sp.dma_start(x_nat[slot][:], x[bass.ds(b, 1)].rearrange("b s d -> (b s) d"))\
                    .then_inc(x_in[slot], 16)

            def load_after(b, slot):
                sp.wait_ge(wc_lo_ready, NS * (b + 1 - SPLIT0))
                sp.wait_ge(xT_lo_ready, b + 1 - SPLIT0)
                sp.wait_ge(raw_chunk_done, b + 1 - SPLIT0)
                load_xT(b + 2, slot)
                load_wc(b + 2, slot)

            def load_residual_after(b, slot):
                sp.wait_ge(xb_ready, b + 1)
                load_x(b + 2, slot)

            def store(b, slot):
                sp.wait_ge(o_ready, b + 1)
                sp.dma_start(out[bass.ds(b, 1)].rearrange("b s d -> (b s) d"), o_sb[slot][:])\
                    .then_inc(stored[slot], 16)

            a0 = sp.value_load(ids[0:1, 0:1], min_val=0, max_val=NADAPT - 1)
            load_xT(0, 0)
            for c in range(C):
                sp.dma_start(wc_raw[0][:, c, :], wcT[bass.ds(a0, 1), :, c, :].rearrange("a p o -> (a p) o"))\
                    .then_inc(wc0_in[c], 16)
            sp.dma_start(az_raw[:], azT).then_inc(az_in, 16)
            load_xT(1, 1)
            load_wc(1, 1)
            sp.dma_start(w_raw[:], wT).then_inc(w_in, 16)
            sp.dma_start(rbias_bc[:], rbias.partition_broadcast(P)).then_inc(rbias_in, 16)
            sp.dma_start(b_raw[:], bT).then_inc(b_in, 16)
            for slot in range(2):
                sp.wait_ge(y_done, slot + 1)
                load_xT(SPLIT0 + slot, slot)
                load_wc(SPLIT0 + slot, slot)
                if slot == 0:
                    sp.dma_start(bias_bc[:], bias.partition_broadcast(P)).then_inc(bias_in, 16)
                load_x(slot, slot)

            with sp.Fori(0, PAIRS - 2) as k:
                for slot in range(2):
                    load_residual_after(2 * k + slot, slot)
                    load_after(2 * k + 2 + slot, slot)
                    store(2 * k + slot, slot)
            for b in range(B - 4, B):
                if b < B - 2:
                    load_residual_after(b, b % 2)
                store(b, b % 2)
            for slot in range(2):
                sp.wait_ge(stored[slot], 16 * PAIRS)

        @block.gpsimd
        def _(pool):
            nc.gpsimd.memset(ident[:], 0.0).then_inc(ident_zeroed, 1)
            nc.gpsimd.memset(mean_w[:], 1.0 / (Q_END - Q_START)).then_inc(mean_set, 1)
            pool.wait_ge(ident_zeroed, 1)
            nc.gpsimd.affine_select(out=ident[:], in_=ident[:], compare_op=ALU.not_equal, fill=1.0, base=0,
                                    pattern=[[-1, P]], channel_multiplier=1).then_inc(ident_ready, 1)
            pool.wait_ge(mean_set, 1)
            nc.gpsimd.affine_select(out=mean_w[:], in_=mean_w[:], compare_op=ALU.is_ge, fill=0.0, base=-Q_START,
                                    pattern=[[0, P]], channel_multiplier=1).then_inc(mean_set, 1)
            pool.wait_ge(mean_set, 2)
            nc.gpsimd.affine_select(out=mean_w[:], in_=mean_w[:], compare_op=ALU.is_ge, fill=0.0,
                                    base=Q_END - 1, pattern=[[0, P]],
                                    channel_multiplier=-1).then_inc(mean_ready, 1)
            pool.wait_ge(b2_ready, 1)
            pool.wait_ge(b_hi_ready, 1)
            nc.gpsimd.tensor_tensor(b_lo[:], b2[:], b_hi[:].bitcast(F32), ALU.subtract).then_inc(b_lo_ready, 1)

            def lo_x(b, slot):
                pool.wait_ge(xT_hi_ready, b + 1 - SPLIT0)
                nc.gpsimd.tensor_tensor(xT_lo[slot][:, 1:C, :], xT_raw[slot][:, 1:C, :],
                                        xT_hi[slot][:, 1:C, :].bitcast(F32), ALU.subtract)\
                    .then_inc(xT_lo_ready, 1)

            def add_bias(k, slot):
                pool.wait_ge(x_in[slot], 16 * (k + 1))
                if not isinstance(k, int):
                    pool.wait_ge(o_ready, 2 * k + slot - 1)
                nc.gpsimd.tensor_tensor(xb[slot][:], x_nat[slot][:], bias_bc[:], ALU.add).then_inc(xb_ready, 1)

            pool.wait_ge(bias_in, 16)
            for slot in range(2):
                add_bias(0, slot)
            with pool.Fori(1, PAIRS) as k:
                for slot in range(2):
                    lo_x(2 * k + slot, slot)
                    add_bias(k, slot)

        @block.scalar
        def _(act):
            copy = nc.scalar.copy

            def copy_y(b):
                act.wait_ge(y_done, b + 1)
                copy(y_sb[:], ps_y[:]).then_inc(y_copied, 1)

            def hi_yT(b):
                act.wait_ge(yT_done, b + 1)
                copy(flat(yT_hi), ps_yT[:]).then_inc(yT_hi_ready, 1)

            def hi_x(k, slot):
                act.wait_ge(xT_in[slot], 16 * (k + 1))
                act.wait_ge(y_done, 2 * k + slot - 1)
                copy(xT_hi[slot][:, 1:C, :], xT_raw[slot][:, 1:C, :]).then_inc(xT_hi_ready, 1)

            def hi_wc(k, slot, c):
                if c == 1:
                    act.wait_ge(wc_in[slot], 16 * (k + slot))
                copy(wc_hi[slot][:, c, :], wc_raw[slot][:, c, :]).then_inc(wc_hi_ready, 1)

            def copy_z(b):
                act.wait_ge(tz_done, b + 1)
                copy(z_sb[:], ps_tz[:, ER:TZ]).then_inc(z_copied, 1)

            def exponent(b):
                act.wait_ge(nmax_ready, b + 1)
                nc.scalar.activation(expd[:], nlogit[:], ACT.Exp, bias=nmax[:], scale=-1.0,
                                     accum_out=esum[:]).then_inc(exp_ready, 1)

            def hi_tsT(b):
                act.wait_ge(tsT_done, b + 1)
                copy(tsT_hi[:], ps_tsT[:, 0:S]).then_inc(tsT_hi_ready, 1)

            def step(k, slot):
                b = 2 * k + slot
                hi_yT(b)
                hi_x(k + 1, slot)
                copy_z(b)
                hi_wc(k + 1, slot, 1)
                exponent(b)
                for c in range(2, C):
                    hi_wc(k + 1, slot, c)
                copy_y(b + 1)
                hi_tsT(b)

            act.wait_ge(az_in, 16)
            copy(az_hi[:], az_raw[:]).then_inc(az_hi_ready, 1)
            copy_y(0)
            hi_yT(0)
            copy_z(0)
            act.wait_ge(w_in, 16)
            for c in range(C):
                copy(w_hi[:, c, :], w_raw[:, c, :]).then_inc(w_hi_ready, 1)
            exponent(0)
            copy_y(1)
            act.wait_ge(b_in, 16)
            nc.scalar.mul(b2[:], b_raw[:], LORA_SCALE).then_inc(b2_ready, 1)
            nc.scalar.mul(b_hi[:], b_raw[:], LORA_SCALE).then_inc(b_hi_ready, 1)
            hi_tsT(0)
            hi_x(1, 0)
            for c in range(1, C):
                hi_wc(1, 0, c)
            step(0, 1)
            with act.Fori(1, PAIRS - 1) as k:
                for slot in range(2):
                    step(k, slot)
            for b in range(B - 2, B):
                hi_yT(b)
                copy_z(b)
                exponent(b)
                if b < B - 1:
                    copy_y(b + 1)
                hi_tsT(b)

        @block.vector
        def _(dve):
            tt = nc.vector.tensor_tensor

            def lo_yT(b):
                dve.wait_ge(yT_hi_ready, b + 1)
                tt(flat(yT_lo), ps_yT[:], flat(yT_hi).bitcast(F32), ALU.subtract).then_inc(yT_lo_ready, 1)

            def lo_wc(b, slot, c):
                dve.wait_ge(wc_hi_ready, NS * (b - SPLIT0) + c)
                tt(wc_lo[slot][:, c, :], wc_raw[slot][:, c, :], wc_hi[slot][:, c, :].bitcast(F32),
                   ALU.subtract).then_inc(wc_lo_ready, 1)

            def negated_logits(b):
                dve.wait_ge(rbias_in, 16)
                dve.wait_ge(logit_done, b + 1)
                nc.vector.tensor_tensor_reduce(nlogit[:], ps_logit[:, 0:E], rbias_bc[:], -1.0, F32_MAX,
                                               ALU.add, ALU.min, nmax[:]).then_inc(nmax_ready, 1)

            def scale_t(b):
                dve.wait_ge(exp_ready, b + 1)
                nc.vector.reciprocal(rsum[:], esum[:]).then_inc(rsum_ready, 1)
                dve.wait_ge(rsum_ready, b + 1)
                nc.vector.scalar_tensor_tensor(
                    out=ts[:].rearrange("p (e r) -> p e r", e=E),
                    in0=ps_tz[:, 0:ER].rearrange("p (e r) -> p e r", e=E), scalar=rsum[:, 0:1],
                    in1=expd[:].unsqueeze(2).to_broadcast([P, E, R]), op0=ALU.mult,
                    op1=ALU.mult).then_inc(ts_ready, 1)

            def lo_tsT(b):
                dve.wait_ge(tsT_hi_ready, b + 1)
                tt(tsT_lo[:], ps_tsT[:, 0:S], tsT_hi[:].bitcast(F32), ALU.subtract).then_inc(tsT_lo_ready, 1)

            def add_residual(k, slot):
                b = 2 * k + slot
                dve.wait_ge(o_done, b + 1)
                dve.wait_ge(xb_ready, b + 1)
                if not (isinstance(k, int) and k == 0):
                    dve.wait_ge(stored[slot], 16 * k)
                tt(o_sb[slot][:], ps_o[slot][:], xb[slot][:], ALU.add).then_inc(o_ready, 1)

            def step(k, slot):
                b = 2 * k + slot
                lo_yT(b)
                add_residual(k - 1 + slot, 1 - slot)
                lo_wc(b + 2, slot, 1)
                negated_logits(b)
                lo_wc(b + 2, slot, 2)
                scale_t(b)
                lo_wc(b + 2, slot, 3)
                lo_tsT(b)

            dve.wait_ge(az_hi_ready, 1)
            tt(az_lo[:], az_raw[:], az_hi[:].bitcast(F32), ALU.subtract).then_inc(az_lo_ready, 1)
            lo_yT(0)
            for c in range(C):
                dve.wait_ge(w_hi_ready, c + 1)
                tt(w_lo[:, c, :], w_raw[:, c, :], w_hi[:, c, :].bitcast(F32), ALU.subtract)\
                    .then_inc(w_lo_ready, 1)
                if c == 1:
                    negated_logits(0)
            scale_t(0)
            lo_tsT(0)
            for c in range(1, C):
                lo_wc(2, 0, c)
            step(0, 1)
            with dve.Fori(1, PAIRS - 1) as k:
                for slot in range(2):
                    step(k, slot)
            for b in range(B - 2, B):
                lo_yT(b)
                add_residual((b - 1) // 2, (b - 1) % 2)
                negated_logits(b)
                scale_t(b)
                lo_tsT(b)
            add_residual(PAIRS - 1, 1)

        @block.tensor
        def _(pe):
            mm = nc.tensor.matmul

            def three(ps, hi_s, lo_s, hi_m, lo_m, start, stop):
                mm(ps, hi_s, hi_m, start=start, stop=False)
                mm(ps, hi_s, lo_m, start=False, stop=False)
                return mm(ps, lo_s, hi_m, start=False, stop=stop)

            def y_raw(slot, c):
                return mm(ps_y[:], xT_raw[slot][:, c, :], wc_raw[slot][:, c, :], start=(c == 0), stop=(c == C - 1))

            def y_split(b, slot, c):
                pe.wait_ge(wc_lo_ready, NS * (b - SPLIT0) + c)
                return three(ps_y[:], xT_hi[slot][:, c, :], xT_lo[slot][:, c, :], wc_hi[slot][:, c, :],
                             wc_lo[slot][:, c, :], False, c == C - 1)

            def transpose_y(b):
                pe.wait_ge(y_copied, b + 1)
                for c in range(C):
                    last = nc.tensor.transpose(ps_yT[:, c * S:(c + 1) * S], y_sb[:, c * P:(c + 1) * P], ident[:])
                last.then_inc(yT_done, 1)

            def t_and_z(b):
                pe.wait_ge(yT_hi_ready, b + 1)
                pe.wait_ge(yT_lo_ready, b + 1)
                for c in range(C):
                    last = three(ps_tz[:, 0:TZ], yT_hi[:, c, :], yT_lo[:, c, :], az_hi[:, c, :], az_lo[:, c, :],
                                 c == 0, c == C - 1)
                last.then_inc(tz_done, 1)

            def logits(b):
                pe.wait_ge(z_copied, b + 1)
                mm(ps_logit[:, 0:E], mean_w[:], z_sb[:], start=True, stop=True).then_inc(logit_done, 1)

            def base(slot, c):
                three(ps_o[slot][:], yT_hi[:, c, :], yT_lo[:, c, :], w_hi[:, c, :], w_lo[:, c, :], c == 0, False)

            def transpose_t(b):
                pe.wait_ge(ts_ready, b + 1)
                nc.tensor.transpose(ps_tsT[:, 0:S], ts[:], ident[:]).then_inc(tsT_done, 1)

            def lora(b, slot):
                pe.wait_ge(tsT_hi_ready, b + 1)
                pe.wait_ge(tsT_lo_ready, b + 1)
                three(ps_o[slot][:], tsT_hi[:], tsT_lo[:], b_hi[:], b_lo[:], False, True).then_inc(o_done, 1)

            def step(k, slot):
                b = 2 * k + slot
                nk, nslot = k + slot, 1 - slot
                pe.wait_ge(xT_in[nslot], 16 * (nk + 1))
                pe.wait_ge(wc_in[nslot], 16 * (nk + nslot))
                y_raw(nslot, 0).then_inc(raw_chunk_done, 1)
                t_and_z(b)
                pe.wait_ge(xT_hi_ready, b + 2 - SPLIT0)
                pe.wait_ge(xT_lo_ready, b + 2 - SPLIT0)
                y_split(b + 1, nslot, 1)
                logits(b)
                y_split(b + 1, nslot, 2)
                y_split(b + 1, nslot, 3).then_inc(y_done, 1)
                if not (isinstance(k, int) and k == 0):
                    pe.wait_ge(o_ready, b - 1)
                for c in range(C - 1):
                    base(slot, c)
                transpose_t(b)
                base(slot, C - 1)
                transpose_y(b + 1)
                lora(b, slot)

            pe.wait_ge(xT_in[0], 16)
            for c in range(C):
                pe.wait_ge(wc0_in[c], 16)
                last = y_raw(0, c)
            last.then_inc(y_done, 1)
            pe.wait_ge(ident_ready, 1)
            transpose_y(0)
            pe.wait_ge(az_hi_ready, 1)
            pe.wait_ge(az_lo_ready, 1)
            t_and_z(0)
            pe.wait_ge(xT_in[1], 16)
            pe.wait_ge(wc_in[1], 16)
            y_raw(1, 0)
            pe.wait_ge(mean_ready, 1)
            logits(0)
            for c in range(1, C):
                last = y_raw(1, c)
            last.then_inc(y_done, 1)
            for c in range(C):
                pe.wait_ge(w_lo_ready, c + 1)
                base(0, c)
            transpose_t(0)
            transpose_y(1)
            pe.wait_ge(b_hi_ready, 1)
            pe.wait_ge(b_lo_ready, 1)
            lora(0, 0)

            step(0, 1)
            with pe.Fori(1, PAIRS - 1) as k:
                for slot in range(2):
                    step(k, slot)
            step(PAIRS - 1, 0)
            t_and_z(B - 1)
            logits(B - 1)
            pe.wait_ge(o_ready, B - 2)
            for c in range(C):
                base(1, c)
            transpose_t(B - 1)
            lora(B - 1, 1)


def kernel(x, itok_B_1_14, L0_cond_weight, L0_ffn_W, L0_ffn_b, L0_ffn_A, L0_ffn_B, L0_ffn_router_W,
           L0_ffn_router_b):
    import numpy as np
    import concourse.bacc as bacc
    from concourse.bass_utils import run_bass_kernel_spmd

    x, wc, w, bias, a, b, rw, rb = (np.asarray(v) for v in (
        x, L0_cond_weight, L0_ffn_W, L0_ffn_b, L0_ffn_A, L0_ffn_B, L0_ffn_router_W, L0_ffn_router_b))
    nb, s, d = x.shape
    c = d // P
    e, r, _ = a.shape

    def contraction_first(m):
        m = np.moveaxis(m.reshape(*m.shape[:-1], c, P), (-1, -2), (-3, -2))
        return np.ascontiguousarray(m)

    arrays = {
        "x": np.ascontiguousarray(x),
        "xT": contraction_first(x),
        "ids": np.ascontiguousarray(np.asarray(itok_B_1_14).reshape(1, nb)),
        "wcT": contraction_first(wc),
        "wT": contraction_first(w),
        "azT": contraction_first(np.concatenate([a.reshape(e * r, d), rw])),
        "bT": np.ascontiguousarray(b.transpose(0, 2, 1).reshape(e * r, d)),
        "bias": np.ascontiguousarray(bias.reshape(1, d)),
        "rbias": np.ascontiguousarray(rb.reshape(1, e)),
    }
    nc = bacc.Bacc("TRN2", target_bir_lowering=False, num_devices=1)
    args = [nc.dram_tensor(f"in_{n}_dram", v.shape, mybir.dt.from_np(v.dtype), kind="ExternalInput").ap()
            for n, v in arrays.items()]
    out = nc.dram_tensor("out_0_dram", x.shape, F32, kind="ExternalOutput").ap()
    adapter_lora_kernel(nc, *args, out)
    got = run_bass_kernel_spmd(nc, [{f"in_{n}_dram": v for n, v in arrays.items()}], core_ids=[0])
    return got.results[0]["out_0_dram"]
```

```python
from contextlib import ExitStack

import concourse.bass as bass
from concourse import mybir

P = 128
F32 = mybir.dt.float32
F32R = mybir.dt.float32r
BF16 = mybir.dt.bfloat16
ALU = mybir.AluOpType
ACT = mybir.ActivationFunctionType

Q_START, Q_END = 107, 127
LORA_SCALE = 2.0


def adapter_lora_kernel(nc, x, xT, ids, wcT, azwT, bT, bias, rbias, out):
    B, S, D = x.shape
    C = D // P
    NADAPT = wcT.shape[0]
    E = rbias.shape[1]
    ER = bT.shape[0]
    R = ER // E
    TZ = ER + E
    HALF = D // 2
    assert S == P and ER == P and C == 4 and B % 2 == 0 and B >= 8

    with ExitStack() as ctx:
        def sb(name, shape, dt=F32):
            return ctx.enter_context(nc.sbuf_tensor(name, shape, dt))

        def psum(name, banks=()):
            return ctx.enter_context(nc.psum_tensor(name, [P, *banks, D], F32))

        def sem(name):
            return ctx.enter_context(nc.semaphore(name))

        xT_raw = sb("xT_raw", [P, B, C, S])
        wc_raw = sb("wc_raw", [P, B, C, D])
        x_res = sb("x_res", [P, B, D])
        xT_hi = sb("xT_hi", [P, C, S], F32R)
        xT_lo = sb("xT_lo", [P, C, S], F32R)
        wc_hi = sb("wc_hi", [P, C, D], F32R)
        wc_lo = sb("wc_lo", [P, C, D], F32R)
        w_raw = sb("w_raw", [P, C, TZ + D])
        w_hi = sb("w_hi", [P, C, TZ + D], F32R)
        w_lo = sb("w_lo", [P, C, TZ + D], F32R)
        b_raw = sb("b_raw", [P, D])
        b2 = sb("b2", [P, D])
        b_hi = sb("b_hi", [P, D], F32R)
        b_lo = sb("b_lo", [P, D], F32R)
        bias_bc = sb("bias_bc", [P, D])
        rbias_bc = sb("rbias_bc", [P, E])
        ident = sb("ident", [P, P])
        mean_w = sb("mean_w", [P, P])
        warm = sb("warm", [P, D], BF16)
        y_sb = sb("y_sb", [P, D])
        yT_hi = [sb(f"yT_hi{p}", [P, C, S], F32R) for p in range(2)]
        yT_lo = [sb(f"yT_lo{p}", [P, C, S], F32R) for p in range(2)]
        z_sb = sb("z_sb", [P, E])
        nlogit = sb("nlogit", [P, E])
        nmax = sb("nmax", [P, 1])
        expd = sb("expd", [P, E])
        esum = sb("esum", [P, 1])
        rsum = sb("rsum", [P, 1])
        ts = sb("ts", [P, ER])
        tsT_hi = sb("tsT_hi", [P, S], F32R)
        tsT_lo = sb("tsT_lo", [P, S], F32R)
        o_sb = [sb(f"o_sb{p}", [P, D]) for p in range(2)]

        ps_y = psum("ps_y")
        ps_yT = psum("ps_yT")
        ps_logit = psum("ps_logit")
        ps_tsT = psum("ps_tsT")
        ps_o = [psum(f"ps_o{p}", (2,)) for p in range(2)]
        BASE = slice(TZ, TZ + HALF)

        xT0_in = [sem(f"xT0_in{n}") for n in range(2)]
        wc0_in = [sem(f"wc0_in{c}") for c in range(C)]
        xT_in = [sem(f"xT_in{p}") for p in range(2)]
        wc_in = [[sem(f"wc_in{p}_{h}") for h in range(2)] for p in range(2)]
        x_in = [sem(f"x_in{p}") for p in range(2)]
        w_in = [sem(f"w_in{c}") for c in range(C)]
        b_in = sem("b_in")
        bias_in = sem("bias_in")
        rbias_in = sem("rbias_in")
        stored = [sem(f"stored{p}") for p in range(2)]
        last_stored = sem("last_stored")
        warm_ready = sem("warm_ready")
        ident_zeroed = sem("ident_zeroed")
        ident_ready = sem("ident_ready")
        mean_set = sem("mean_set")
        mean_ready = sem("mean_ready")
        w_hi_ready = sem("w_hi_ready")
        w_lo_ready = sem("w_lo_ready")
        b2_ready = sem("b2_ready")
        b_hi_ready = sem("b_hi_ready")
        b_lo_ready = sem("b_lo_ready")
        y_done = sem("y_done")
        yT_done = sem("yT_done")
        tzb_done = sem("tzb_done")
        logit_done = sem("logit_done")
        tsT_done = sem("tsT_done")
        o_done = sem("o_done")
        xb_ready = sem("xb_ready")
        y_copied = sem("y_copied")
        yT_hi_ready = sem("yT_hi_ready")
        yT_lo_ready = sem("yT_lo_ready")
        z_copied = sem("z_copied")
        nlogit_ready = sem("nlogit_ready")
        nmax_ready = sem("nmax_ready")
        exp_ready = sem("exp_ready")
        rsum_ready = sem("rsum_ready")
        ts_ready = sem("ts_ready")
        tsT_hi_ready = sem("tsT_hi_ready")
        tsT_lo_ready = sem("tsT_lo_ready")
        o_ready = sem("o_ready")
        xT_hi_ready = sem("xT_hi_ready")
        xT_lo_ready = sem("xT_lo_ready")
        wc_hi_ready = sem("wc_hi_ready")
        wc_lo_ready = sem("wc_lo_ready")

        PAIRS = B // 2
        CH = C // 2
        SPLIT0 = 3
        WARM_UPS, WARM_COPY = 9, 3

        def flat(t):
            return t[:].rearrange("p c s -> p (c s)")

        def half(t, h):
            return t[:, CH * h:CH * (h + 1), :].rearrange("p c s -> p (c s)")

        def halves_split(b, h):
            return 2 * (b - SPLIT0) + h + 1

        def raw_half(b, h):
            return wc_raw[:, bass.ds(b, 1), CH * h:CH * (h + 1), :].rearrange("p b c o -> p (b c o)")

        def raw_x(b):
            return xT_raw[:, bass.ds(b, 1)].rearrange("p b c s -> p (b c s)")

        block = ctx.enter_context(nc.Block())

        @block.sync
        def _(sp):
            def adapter_of(b):
                return sp.value_load(ids[0:1, bass.ds(b, 1)], min_val=0, max_val=NADAPT - 1)

            def load_batch(k, slot, landed):
                b = 2 * k + slot
                a = adapter_of(b)
                if landed is not None:
                    sp.wait_ge(xT_in[slot], 16 * landed)
                    sp.wait_ge(wc_in[slot][0], 16 * landed)
                    sp.wait_ge(wc_in[slot][1], 16 * landed)
                sp.dma_start(raw_x(b), xT[bass.ds(b, 1)].rearrange("b p c s -> (b p) (c s)"))\
                    .then_inc(xT_in[slot], 16)
                for h in range(2):
                    sp.dma_start(raw_half(b, h),
                                 wcT[bass.ds(a, 1), :, CH * h:CH * (h + 1), :].rearrange("a p c o -> (a p) (c o)"))\
                        .then_inc(wc_in[slot][h], 16)

            def load_residual(k, slot):
                b = 2 * k + slot
                if not (isinstance(k, int) and k == 0):
                    sp.wait_ge(x_in[slot], 16 * k)
                sp.dma_start(x_res[:, bass.ds(b, 1)].rearrange("p b d -> p (b d)"),
                             x[bass.ds(b, 1)].rearrange("b s d -> (b s) d")).then_inc(x_in[slot], 16)

            def store(b, slot):
                sp.wait_ge(o_ready, b + 1)
                sp.dma_start(out[bass.ds(b, 1)].rearrange("b s d -> (b s) d"), o_sb[slot][:])\
                    .then_inc(stored[slot], 16)

            a = adapter_of(0)
            for c in range(C):
                if c < 2:
                    part = slice(0, 1) if c == 0 else slice(1, C)
                    sp.dma_start(xT_raw[:, 0, part, :], xT[0, :, part, :]).then_inc(xT0_in[c], 16)
                sp.dma_start(wc_raw[:, 0, c, :], wcT[bass.ds(a, 1), :, c, :].rearrange("a p o -> (a p) o"))\
                    .then_inc(wc0_in[c], 16)
            load_batch(0, 1, None)
            for c in range(C):
                sp.dma_start(w_raw[:, c, :], azwT[:, c, :]).then_inc(w_in[c], 16)
            sp.dma_start(rbias_bc[:], rbias.partition_broadcast(P)).then_inc(rbias_in, 16)
            load_batch(1, 0, None)
            sp.dma_start(b_raw[:], bT).then_inc(b_in, 16)
            load_batch(1, 1, 1)
            sp.dma_start(bias_bc[:], bias.partition_broadcast(P)).then_inc(bias_in, 16)
            load_residual(0, 0)
            load_residual(0, 1)
            with sp.Fori(2, PAIRS) as k:
                for slot in range(2):
                    load_batch(k, slot, k + slot - 1)
                    load_residual(k - 1, slot)
            for slot in range(2):
                load_residual(PAIRS - 1, slot)
            store(B - 3, 1)
            store(B - 2, 0)
            for n in range(2):
                sp.wait_ge(o_ready, B + n)
                sp.dma_start(out[B - 1, :, n * HALF:(n + 1) * HALF], o_sb[1][:, n * HALF:(n + 1) * HALF])\
                    .then_inc(stored[1] if n == 0 else last_stored, 16)
            for slot in range(2):
                sp.wait_ge(stored[slot], 16 * PAIRS)
            sp.wait_ge(last_stored, 16)

        @block.gpsimd
        def _(pool):
            nc.gpsimd.memset(ident[:], 0.0).then_inc(ident_zeroed, 1)
            nc.gpsimd.memset(mean_w[:], 1.0 / (Q_END - Q_START)).then_inc(mean_set, 1)
            pool.wait_ge(ident_zeroed, 1)
            nc.gpsimd.affine_select(out=ident[:], in_=ident[:], compare_op=ALU.not_equal, fill=1.0, base=0,
                                    pattern=[[-1, P]], channel_multiplier=1).then_inc(ident_ready, 1)
            pool.wait_ge(mean_set, 1)
            nc.gpsimd.affine_select(out=mean_w[:], in_=mean_w[:], compare_op=ALU.is_ge, fill=0.0, base=-Q_START,
                                    pattern=[[0, P]], channel_multiplier=1).then_inc(mean_set, 1)
            pool.wait_ge(mean_set, 2)
            nc.gpsimd.affine_select(out=mean_w[:], in_=mean_w[:], compare_op=ALU.is_ge, fill=0.0,
                                    base=Q_END - 1, pattern=[[0, P]],
                                    channel_multiplier=-1).then_inc(mean_ready, 1)

            def lo_x(b):
                pool.wait_ge(xT_hi_ready, b - SPLIT0 + 1)
                nc.gpsimd.tensor_tensor(flat(xT_lo), raw_x(b), flat(xT_hi).bitcast(F32), ALU.subtract)\
                    .then_inc(xT_lo_ready, 1)

            def add_bias(k, slot):
                pool.wait_ge(x_in[slot], 16 * (k + 1))
                x_b = x_res[:, bass.ds(2 * k + slot, 1)].rearrange("p b d -> p (b d)")
                nc.gpsimd.tensor_tensor(x_b, x_b, bias_bc[:], ALU.add).then_inc(xb_ready, 1)

            pool.wait_ge(b2_ready, 1)
            pool.wait_ge(b_hi_ready, 1)
            nc.gpsimd.tensor_tensor(b_lo[:], b2[:], b_hi[:].bitcast(F32), ALU.subtract).then_inc(b_lo_ready, 1)
            pool.wait_ge(bias_in, 16)
            add_bias(0, 0)
            with pool.Fori(0, PAIRS - 2) as k:
                lo_x(2 * k + 3)
                add_bias(k, 1)
                lo_x(2 * k + 4)
                add_bias(k + 1, 0)
            lo_x(B - 1)
            add_bias(PAIRS - 2, 1)
            for slot in range(2):
                add_bias(PAIRS - 1, slot)

        @block.scalar
        def _(act):
            copy = nc.scalar.copy

            def hi_w(c):
                act.wait_ge(w_in[c], 16)
                copy(w_hi[:, c, :], w_raw[:, c, :]).then_inc(w_hi_ready, 1)

            def copy_y(b):
                act.wait_ge(y_done, b + 1)
                copy(y_sb[:], ps_y[:]).then_inc(y_copied, 1)

            def hi_yT(b, slot):
                act.wait_ge(yT_done, b + 1)
                copy(flat(yT_hi[slot]), ps_yT[:]).then_inc(yT_hi_ready, 1)

            def hi_x(k, slot):
                act.wait_ge(xT_in[slot], 16 * (k + slot))
                copy(flat(xT_hi), raw_x(2 * k + slot)).then_inc(xT_hi_ready, 1)

            def hi_wc(k, slot, h):
                act.wait_ge(wc_in[slot][h], 16 * (k + slot))
                copy(half(wc_hi, h), raw_half(2 * k + slot, h)).then_inc(wc_hi_ready, 1)

            def copy_z(b, bank):
                act.wait_ge(tzb_done, b + 1)
                copy(z_sb[:], bank[:, ER:TZ]).then_inc(z_copied, 1)

            def exponent(b):
                act.wait_ge(nmax_ready, b + 1)
                nc.scalar.activation(expd[:], nlogit[:], ACT.Exp, bias=nmax[:], scale=-1.0,
                                     accum_out=esum[:]).then_inc(exp_ready, 1)

            def hi_tsT(b):
                act.wait_ge(tsT_done, b + 1)
                copy(tsT_hi[:], ps_tsT[:, 0:S]).then_inc(tsT_hi_ready, 1)

            def store(b, slot):
                act.wait_ge(o_ready, b + 1)
                act.dma_start(out[bass.ds(b, 1)].rearrange("b s d -> (b s) d"), o_sb[slot][:])\
                    .then_inc(stored[slot], 16)

            def step(k, slot):
                b = 2 * k + slot
                hi_tsT(b - 1)
                copy_y(b + 1)
                hi_x(k + 1, slot)
                for h in range(2):
                    hi_wc(k + 1, slot, h)
                store(b - 1, 1 - slot)
                hi_yT(b + 1, 1 - slot)
                copy_z(b, ps_o[slot][:, 0])
                exponent(b)

            copy_y(0)
            hi_yT(0, 0)
            hi_w(0)
            hi_w(1)
            copy_y(1)
            hi_w(2)
            hi_w(3)
            hi_yT(1, 1)
            copy_z(0, ps_o[0][:, 0])
            exponent(0)
            act.wait_ge(b_in, 16)
            nc.scalar.mul(b2[:], b_raw[:], LORA_SCALE).then_inc(b2_ready, 1)
            nc.scalar.mul(b_hi[:], b_raw[:], LORA_SCALE).then_inc(b_hi_ready, 1)
            with act.Fori(0, PAIRS - 2) as k:
                step(k, 1)
                step(k + 1, 0)
            step(PAIRS - 2, 1)
            hi_tsT(B - 3)
            copy_y(B - 1)
            hi_yT(B - 1, 1)
            copy_z(B - 2, ps_o[0][:, 0])
            exponent(B - 2)
            copy_z(B - 1, ps_y)
            hi_tsT(B - 2)
            exponent(B - 1)
            hi_tsT(B - 1)

        @block.vector
        def _(dve):
            tt = nc.vector.tensor_tensor

            def lo_w(c):
                dve.wait_ge(w_hi_ready, c + 1)
                tt(w_lo[:, c, :], w_raw[:, c, :], w_hi[:, c, :].bitcast(F32), ALU.subtract)\
                    .then_inc(w_lo_ready, 1)

            def lo_yT(b, slot):
                dve.wait_ge(yT_hi_ready, b + 1)
                tt(flat(yT_lo[slot]), ps_yT[:], flat(yT_hi[slot]).bitcast(F32), ALU.subtract)\
                    .then_inc(yT_lo_ready, 1)

            def lo_wc(b, h):
                dve.wait_ge(wc_hi_ready, halves_split(b, h))
                tt(half(wc_lo, h), raw_half(b, h), half(wc_hi, h).bitcast(F32), ALU.subtract)\
                    .then_inc(wc_lo_ready, 1)

            def negated_logits(b):
                dve.wait_ge(logit_done, b + 1)
                nc.vector.scalar_tensor_tensor(out=nlogit[:], in0=ps_logit[:, 0:E], scalar=-1.0, in1=rbias_bc[:],
                                               op0=ALU.mult, op1=ALU.subtract).then_inc(nlogit_ready, 1)
                dve.wait_ge(nlogit_ready, b + 1)
                nc.vector.tensor_reduce(nmax[:], nlogit[:], mybir.AxisListType.X, ALU.min).then_inc(nmax_ready, 1)

            def scale_t(b, bank):
                dve.wait_ge(exp_ready, b + 1)
                nc.vector.reciprocal(rsum[:], esum[:]).then_inc(rsum_ready, 1)
                dve.wait_ge(rsum_ready, b + 1)
                nc.vector.scalar_tensor_tensor(
                    out=ts[:].rearrange("p (e r) -> p e r", e=E),
                    in0=bank[:, 0:ER].rearrange("p (e r) -> p e r", e=E), scalar=rsum[:, 0:1],
                    in1=expd[:].unsqueeze(2).to_broadcast([P, E, R]), op0=ALU.mult,
                    op1=ALU.mult).then_inc(ts_ready, 1)

            def lo_tsT(b):
                dve.wait_ge(tsT_hi_ready, b + 1)
                tt(tsT_lo[:], ps_tsT[:, 0:S], tsT_hi[:].bitcast(F32), ALU.subtract).then_inc(tsT_lo_ready, 1)

            def add_residual(k, slot):
                b = 2 * k + slot
                dve.wait_ge(o_done, b + 1)
                dve.wait_ge(xb_ready, b + 1)
                if not (isinstance(k, int) and k == 0):
                    dve.wait_ge(stored[slot], 16 * k)
                tt(o_sb[slot][:].rearrange("p (n h) -> p n h", n=2), ps_o[slot][:, :, BASE],
                   x_res[:, bass.ds(b, 1)].rearrange("p b (n h) -> p (b n) h", n=2), ALU.add)\
                    .then_inc(o_ready, 1)

            def step(k, slot):
                b = 2 * k + slot
                lo_tsT(b - 1)
                add_residual(k - 1 + slot, 1 - slot)
                for h in range(2):
                    lo_wc(b + 2, h)
                negated_logits(b)
                scale_t(b, ps_o[slot][:, 0])
                lo_yT(b + 1, 1 - slot)

            nc.vector.memset(warm[:], 0.0).then_inc(warm_ready, 1)
            lo_yT(0, 0)
            for c in range(C):
                lo_w(c)
            lo_yT(1, 1)
            dve.wait_ge(rbias_in, 16)
            negated_logits(0)
            scale_t(0, ps_o[0][:, 0])
            step(0, 1)
            with dve.Fori(1, PAIRS - 1) as k:
                for slot in range(2):
                    step(k, slot)
            lo_tsT(B - 3)
            add_residual(PAIRS - 2, 1)
            lo_yT(B - 1, 1)
            negated_logits(B - 2)
            scale_t(B - 2, ps_o[0][:, 0])
            negated_logits(B - 1)
            lo_tsT(B - 2)
            scale_t(B - 1, ps_y)
            lo_tsT(B - 1)
            add_residual(PAIRS - 1, 0)
            dve.wait_ge(xb_ready, B)
            dve.wait_ge(stored[1], 16 * (PAIRS - 1))
            for n in range(2):
                dve.wait_ge(o_done, B + n)
                half_n = slice(n * HALF, (n + 1) * HALF)
                tt(o_sb[1][:, half_n], ps_o[1][:, n, BASE], x_res[:, B - 1, half_n], ALU.add).then_inc(o_ready, 1)

        @block.tensor
        def _(pe):
            mm = nc.tensor.matmul

            def keep_warm(n):
                for _ in range(n):
                    mm(ps_logit[:], warm[:, 0:P], warm[:], start=True, stop=True)

            def y_raw(b, c):
                last = mm(ps_y[:], xT_raw[:, b, c, :], wc_raw[:, b, c, :], start=(c == 0), stop=(c == C - 1))
                if c == C - 1:
                    last.then_inc(y_done, 1)

            def y_arrived(b, c):
                if c == 0:
                    pe.wait_ge(xT_in[b % 2], 16)
                if c % CH == 0:
                    pe.wait_ge(wc_in[b % 2][c // CH], 16)

            def y_split(b, c):
                if c == 0:
                    pe.wait_ge(xT_lo_ready, b - SPLIT0 + 1)
                if c % CH == 0:
                    pe.wait_ge(wc_lo_ready, halves_split(b, c // CH))
                mm(ps_y[:], xT_hi[:, c, :], wc_hi[:, c, :], start=(c == 0), stop=False)
                mm(ps_y[:], xT_hi[:, c, :], wc_lo[:, c, :], start=False, stop=False)
                last = mm(ps_y[:], xT_lo[:, c, :], wc_hi[:, c, :], start=False, stop=(c == C - 1))
                if c == C - 1:
                    last.then_inc(y_done, 1)

            def transpose_y(b):
                pe.wait_ge(y_copied, b + 1)
                for c in range(C):
                    last = nc.tensor.transpose(ps_yT[:, c * S:(c + 1) * S], y_sb[:, c * P:(c + 1) * P], ident[:])
                last.then_inc(yT_done, 1)

            FIRST = (slice(0, TZ + HALF), 0, slice(0, TZ + HALF))
            SECOND = (slice(TZ + HALF, TZ + D), 1, BASE)

            def products(b, slot, c, parts, banks):
                for stat, mov, n in ((yT_hi, w_hi, 0), (yT_hi, w_lo, 1), (yT_lo, w_hi, 2)):
                    for cols, bank, to in parts:
                        last = mm(banks[:, bank, to], stat[slot][:, c, :], mov[:, c, cols],
                                  start=(c == 0 and n == 0), stop=(c == C - 1 and n == 2))
                return last

            def wait_yT(b):
                pe.wait_ge(yT_hi_ready, b + 1)
                pe.wait_ge(yT_lo_ready, b + 1)

            def logits(b):
                pe.wait_ge(z_copied, b + 1)
                mm(ps_logit[:, 0:E], mean_w[:], z_sb[:], start=True, stop=True).then_inc(logit_done, 1)

            def transpose_t(b):
                pe.wait_ge(ts_ready, b + 1)
                nc.tensor.transpose(ps_tsT[:, 0:S], ts[:], ident[:]).then_inc(tsT_done, 1)

            def lora(b, slot, by_halves=False):
                pe.wait_ge(tsT_hi_ready, b + 1)
                pe.wait_ge(tsT_lo_ready, b + 1)
                for n in range(2):
                    for stat, mov in ((tsT_hi, b_hi), (tsT_hi, b_lo), (tsT_lo, b_hi)):
                        last = mm(ps_o[slot][:, n, BASE], stat[:], mov[:, n * HALF:(n + 1) * HALF], start=False,
                                  stop=False, skip_group_check=True)
                    if by_halves or n == 1:
                        last.then_inc(o_done, 1)

            def step(k, slot, y_ahead=True):
                b = 2 * k + slot
                wait_yT(b)
                if not (isinstance(k, int) and k == 0):
                    pe.wait_ge(o_ready, b - 1)
                products(b, slot, 0, (FIRST, SECOND), ps_o[slot])
                lora(b - 1, 1 - slot)
                products(b, slot, 1, (FIRST, SECOND), ps_o[slot])
                transpose_y(b + 1)
                products(b, slot, 2, (FIRST, SECOND), ps_o[slot])
                products(b, slot, 3, (FIRST, SECOND), ps_o[slot]).then_inc(tzb_done, 1)
                if y_ahead:
                    y_split(b + 2, 0)
                    logits(b)
                    for c in range(1, C):
                        y_split(b + 2, c)
                    transpose_t(b)

            pe.wait_ge(warm_ready, 1)
            keep_warm(WARM_UPS)
            for c in range(C):
                if c < 2:
                    pe.wait_ge(xT0_in[c], 16)
                pe.wait_ge(wc0_in[c], 16)
                y_raw(0, c)
            keep_warm(WARM_COPY)
            pe.wait_ge(ident_ready, 1)
            transpose_y(0)
            for c in range(C):
                y_arrived(1, c)
                y_raw(1, c)
            wait_yT(0)
            for c in range(C):
                pe.wait_ge(w_lo_ready, c + 1)
                last = products(0, 0, c, (FIRST, SECOND), ps_o[0])
                if c == 1:
                    transpose_y(1)
            last.then_inc(tzb_done, 1)
            for c in range(C):
                y_arrived(2, c)
                y_raw(2, c)
                if c == 0:
                    pe.wait_ge(mean_ready, 1)
                    logits(0)
            transpose_t(0)
            pe.wait_ge(b_hi_ready, 1)
            pe.wait_ge(b_lo_ready, 1)

            step(0, 1)
            with pe.Fori(1, PAIRS - 1) as k:
                for slot in range(2):
                    step(k, slot)
            step(PAIRS - 1, 0, y_ahead=False)

            last_slot = 1
            wait_yT(B - 1)
            for c in range(C):
                last = products(B - 1, last_slot, c, ((slice(0, TZ), 0, slice(0, TZ)),),
                                ps_y[:].unsqueeze(1))
            last.then_inc(tzb_done, 1)
            logits(B - 2)
            pe.wait_ge(o_ready, B - 2)
            base = ((slice(TZ, TZ + HALF), 0, BASE), SECOND)
            products(B - 1, last_slot, 0, base, ps_o[last_slot])
            logits(B - 1)
            products(B - 1, last_slot, 1, base, ps_o[last_slot])
            transpose_t(B - 2)
            products(B - 1, last_slot, 2, base, ps_o[last_slot])
            lora(B - 2, 0)
            transpose_t(B - 1)
            products(B - 1, last_slot, 3, base, ps_o[last_slot])
            lora(B - 1, last_slot, by_halves=True)


def kernel(x, itok_B_1_14, L0_cond_weight, L0_ffn_W, L0_ffn_b, L0_ffn_A, L0_ffn_B, L0_ffn_router_W,
           L0_ffn_router_b):
    import numpy as np
    import concourse.bacc as bacc
    from concourse.bass_utils import run_bass_kernel_spmd

    x, wc, w, bias, a, b, rw, rb = (np.asarray(v) for v in (
        x, L0_cond_weight, L0_ffn_W, L0_ffn_b, L0_ffn_A, L0_ffn_B, L0_ffn_router_W, L0_ffn_router_b))
    nb, s, d = x.shape
    c = d // P
    e, r, _ = a.shape

    def contraction_first(m):
        m = np.moveaxis(m.reshape(*m.shape[:-1], c, P), (-1, -2), (-3, -2))
        return np.ascontiguousarray(m)

    arrays = {
        "x": np.ascontiguousarray(x),
        "xT": contraction_first(x),
        "ids": np.ascontiguousarray(np.asarray(itok_B_1_14).reshape(1, nb)),
        "wcT": contraction_first(wc),
        "azwT": contraction_first(np.concatenate([a.reshape(e * r, d), rw, w])),
        "bT": np.ascontiguousarray(b.transpose(0, 2, 1).reshape(e * r, d)),
        "bias": np.ascontiguousarray(bias.reshape(1, d)),
        "rbias": np.ascontiguousarray(rb.reshape(1, e)),
    }
    nc = bacc.Bacc("TRN2", target_bir_lowering=False, num_devices=1)
    args = [nc.dram_tensor(f"in_{n}_dram", v.shape, mybir.dt.from_np(v.dtype), kind="ExternalInput").ap()
            for n, v in arrays.items()]
    out = nc.dram_tensor("out_0_dram", x.shape, F32, kind="ExternalOutput").ap()
    adapter_lora_kernel(nc, *args, out)
    got = run_bass_kernel_spmd(nc, [{f"in_{n}_dram": v for n, v in arrays.items()}], core_ids=[0])
    return got.results[0]["out_0_dram"]
```

```python
from contextlib import ExitStack

import concourse.bass as bass
from concourse import mybir

P = 128
F32 = mybir.dt.float32
F32R = mybir.dt.float32r
BF16 = mybir.dt.bfloat16
ALU = mybir.AluOpType
ACT = mybir.ActivationFunctionType

Q_START, Q_END = 107, 127
LORA_SCALE = 2.0


def adapter_lora_kernel(nc, x, xT, ids, wcT, azwT, bT, bias, rbias, out):
    B, S, D = x.shape
    C = D // P
    NADAPT = wcT.shape[0]
    E = rbias.shape[1]
    ER = bT.shape[0]
    R = ER // E
    TZ = ER + E
    HALF = D // 2
    assert S == P and ER == P and C == 4 and B % 2 == 0 and B >= 8

    with ExitStack() as ctx:
        def sb(name, shape, dt=F32):
            return ctx.enter_context(nc.sbuf_tensor(name, shape, dt))

        def psum(name, banks=()):
            return ctx.enter_context(nc.psum_tensor(name, [P, *banks, D], F32))

        def sem(name):
            return ctx.enter_context(nc.semaphore(name))

        xT_raw = sb("xT_raw", [P, B, C, S])
        wc_raw = sb("wc_raw", [P, B, C, D])
        x_res = sb("x_res", [P, B, D])
        xT_hi = sb("xT_hi", [P, C, S], F32R)
        xT_lo = sb("xT_lo", [P, C, S], F32R)
        wc_hi = sb("wc_hi", [P, C, D], F32R)
        wc_lo = sb("wc_lo", [P, C, D], F32R)
        w_raw = sb("w_raw", [P, C, TZ + D])
        w_hi = sb("w_hi", [P, C, TZ + D], F32R)
        w_lo = sb("w_lo", [P, C, TZ + D], F32R)
        b_raw = sb("b_raw", [P, D])
        b_hi = sb("b_hi", [P, D], F32R)
        b_lo = sb("b_lo", [P, D], F32R)
        bias_bc = sb("bias_bc", [P, D])
        rbias_bc = sb("rbias_bc", [P, E])
        ident = sb("ident", [P, P])
        mean_w = sb("mean_w", [P, P])
        warm = sb("warm", [P, D], BF16)
        y_sb = sb("y_sb", [P, D])
        yT_hi = [sb(f"yT_hi{p}", [P, C, S], F32R) for p in range(2)]
        yT_lo = [sb(f"yT_lo{p}", [P, C, S], F32R) for p in range(2)]
        z_sb = sb("z_sb", [P, E])
        nlogit = sb("nlogit", [P, E])
        nmax = sb("nmax", [P, 1])
        expd = sb("expd", [P, E])
        esum = sb("esum", [P, 1])
        rsum = sb("rsum", [P, 1])
        ts = sb("ts", [P, ER])
        tsT_hi = sb("tsT_hi", [P, S], F32R)
        tsT_lo = sb("tsT_lo", [P, S], F32R)
        o_sb = [sb(f"o_sb{p}", [P, D]) for p in range(2)]

        ps_y = psum("ps_y")
        ps_yT = psum("ps_yT")
        ps_logit = psum("ps_logit")
        ps_tsT = psum("ps_tsT")
        ps_o = [psum(f"ps_o{p}", (2,)) for p in range(2)]
        BASE = slice(TZ, TZ + HALF)

        xT0_in = [sem(f"xT0_in{n}") for n in range(2)]
        x1_in = sem("x1_in")
        wc01_in = [[sem(f"wc{b}_in{c}") for c in range(C)] for b in range(2)]
        xT_in = [sem(f"xT_in{p}") for p in range(2)]
        wc_in = [[sem(f"wc_in{p}_{h}") for h in range(2)] for p in range(2)]
        x_in = [sem(f"x_in{p}") for p in range(2)]
        w_in = [sem(f"w_in{c}") for c in range(C)]
        b_in = sem("b_in")
        bias_in = sem("bias_in")
        rbias_in = sem("rbias_in")
        stored = [sem(f"stored{p}") for p in range(2)]
        last_stored = sem("last_stored")
        warm_ready = sem("warm_ready")
        ident_zeroed = sem("ident_zeroed")
        ident_ready = sem("ident_ready")
        mean_set = sem("mean_set")
        mean_ready = sem("mean_ready")
        w_hi_ready = sem("w_hi_ready")
        w_lo_ready = sem("w_lo_ready")
        b_hi_ready = sem("b_hi_ready")
        b_lo_ready = sem("b_lo_ready")
        y_done = sem("y_done")
        yT_done = sem("yT_done")
        tzb_done = sem("tzb_done")
        logit_done = sem("logit_done")
        tsT_done = sem("tsT_done")
        o_done = sem("o_done")
        xb_ready = sem("xb_ready")
        y_copied = sem("y_copied")
        yT_hi_ready = sem("yT_hi_ready")
        yT_lo_ready = sem("yT_lo_ready")
        z_copied = sem("z_copied")
        nlogit_ready = sem("nlogit_ready")
        nmax_ready = sem("nmax_ready")
        exp_ready = sem("exp_ready")
        rsum_ready = sem("rsum_ready")
        ts_ready = sem("ts_ready")
        tsT_hi_ready = sem("tsT_hi_ready")
        tsT_lo_ready = sem("tsT_lo_ready")
        o_ready = sem("o_ready")
        xT_hi_ready = sem("xT_hi_ready")
        xT_lo_ready = sem("xT_lo_ready")
        wc_hi_ready = sem("wc_hi_ready")
        wc_lo_ready = sem("wc_lo_ready")

        PAIRS = B // 2
        CH = C // 2
        SPLIT0 = 3
        WARM_UPS = 9

        def flat(t):
            return t[:].rearrange("p c s -> p (c s)")

        def half(t, h):
            return t[:, CH * h:CH * (h + 1), :].rearrange("p c s -> p (c s)")

        def halves_split(b, h):
            return 2 * (b - SPLIT0) + h + 1

        def raw_half(b, h):
            return wc_raw[:, bass.ds(b, 1), CH * h:CH * (h + 1), :].rearrange("p b c o -> p (b c o)")

        def raw_x(b):
            return xT_raw[:, bass.ds(b, 1)].rearrange("p b c s -> p (b c s)")

        block = ctx.enter_context(nc.Block())

        @block.sync
        def _(sp):
            def adapter_of(b):
                return sp.value_load(ids[0:1, bass.ds(b, 1)], min_val=0, max_val=NADAPT - 1)

            def load_batch(k, slot, landed=None):
                b = 2 * k + slot
                a = adapter_of(b)
                if landed is not None:
                    sp.wait_ge(xT_in[slot], 16 * landed)
                    sp.wait_ge(wc_in[slot][0], 16 * landed)
                    sp.wait_ge(wc_in[slot][1], 16 * landed)
                sp.dma_start(raw_x(b), xT[bass.ds(b, 1)].rearrange("b p c s -> (b p) (c s)"))\
                    .then_inc(xT_in[slot], 16)
                for h in range(2):
                    sp.dma_start(raw_half(b, h),
                                 wcT[bass.ds(a, 1), :, CH * h:CH * (h + 1), :].rearrange("a p c o -> (a p) (c o)"))\
                        .then_inc(wc_in[slot][h], 16)

            def load_residual(k, slot):
                b = 2 * k + slot
                if not (isinstance(k, int) and k == 0):
                    sp.wait_ge(x_in[slot], 16 * k)
                sp.dma_start(x_res[:, bass.ds(b, 1)].rearrange("p b d -> p (b d)"),
                             x[bass.ds(b, 1)].rearrange("b s d -> (b s) d")).then_inc(x_in[slot], 16)

            def store(b, slot):
                sp.wait_ge(o_ready, b + 1)
                sp.dma_start(out[bass.ds(b, 1)].rearrange("b s d -> (b s) d"), o_sb[slot][:])\
                    .then_inc(stored[slot], 16)

            for b in range(2):
                a = adapter_of(b)
                for c in range(C):
                    sp.dma_start(wc_raw[:, b, c, :], wcT[bass.ds(a, 1), :, c, :].rearrange("a p o -> (a p) o"))\
                        .then_inc(wc01_in[b][c], 16)
            for c in range(C):
                sp.dma_start(w_raw[:, c, :], azwT[:, c, :]).then_inc(w_in[c], 16)
            sp.dma_start(rbias_bc[:], rbias.partition_broadcast(P)).then_inc(rbias_in, 16)
            load_batch(1, 0)
            sp.dma_start(b_raw[:], bT).then_inc(b_in, 16)
            load_batch(1, 1)
            sp.dma_start(bias_bc[:], bias.partition_broadcast(P)).then_inc(bias_in, 16)
            load_residual(0, 0)
            load_residual(0, 1)
            with sp.Fori(2, PAIRS) as k:
                for slot in range(2):
                    load_batch(k, slot, k - 1)
                    load_residual(k - 1, slot)
            for slot in range(2):
                load_residual(PAIRS - 1, slot)
            store(B - 3, 1)
            store(B - 2, 0)
            for n in range(2):
                sp.wait_ge(o_ready, B + n)
                sp.dma_start(out[B - 1, :, n * HALF:(n + 1) * HALF], o_sb[1][:, n * HALF:(n + 1) * HALF])\
                    .then_inc(stored[1] if n == 0 else last_stored, 16)
            for slot in range(2):
                sp.wait_ge(stored[slot], 16 * PAIRS)
            sp.wait_ge(last_stored, 16)

        @block.gpsimd
        def _(pool):
            nc.gpsimd.memset(ident[:], 0.0).then_inc(ident_zeroed, 1)
            nc.gpsimd.memset(mean_w[:], 1.0 / (Q_END - Q_START)).then_inc(mean_set, 1)
            pool.wait_ge(ident_zeroed, 1)
            nc.gpsimd.affine_select(out=ident[:], in_=ident[:], compare_op=ALU.not_equal, fill=1.0, base=0,
                                    pattern=[[-1, P]], channel_multiplier=1).then_inc(ident_ready, 1)
            pool.wait_ge(mean_set, 1)
            nc.gpsimd.affine_select(out=mean_w[:], in_=mean_w[:], compare_op=ALU.is_ge, fill=0.0, base=-Q_START,
                                    pattern=[[0, P]], channel_multiplier=1).then_inc(mean_set, 1)
            pool.wait_ge(mean_set, 2)
            nc.gpsimd.affine_select(out=mean_w[:], in_=mean_w[:], compare_op=ALU.is_ge, fill=0.0,
                                    base=Q_END - 1, pattern=[[0, P]],
                                    channel_multiplier=-1).then_inc(mean_ready, 1)

            def lo_x(b):
                pool.wait_ge(xT_hi_ready, b - SPLIT0 + 1)
                nc.gpsimd.tensor_tensor(flat(xT_lo), raw_x(b), flat(xT_hi).bitcast(F32), ALU.subtract)\
                    .then_inc(xT_lo_ready, 1)

            def add_bias(k, slot):
                pool.wait_ge(x_in[slot], 16 * (k + 1))
                pool.wait_ge(bias_in, 16)
                x_b = x_res[:, bass.ds(2 * k + slot, 1)].rearrange("p b d -> p (b d)")
                nc.gpsimd.tensor_tensor(x_b, x_b, bias_bc[:], ALU.add).then_inc(xb_ready, 1)

            with pool.Fori(0, PAIRS - 2) as k:
                for slot in range(2):
                    lo_x(2 * k + slot + SPLIT0)
                    add_bias(k, slot)
            lo_x(B - 1)
            for slot in range(2):
                add_bias(PAIRS - 2, slot)
            for slot in range(2):
                add_bias(PAIRS - 1, slot)

        @block.scalar
        def _(act):
            copy = nc.scalar.copy

            def hi_w(c):
                act.wait_ge(w_in[c], 16)
                copy(w_hi[:, c, :], w_raw[:, c, :]).then_inc(w_hi_ready, 1)

            def copy_y(b, bank):
                act.wait_ge(y_done, b + 1)
                copy(y_sb[:], bank).then_inc(y_copied, 1)

            def hi_yT(b, slot):
                act.wait_ge(yT_done, b + 1)
                copy(flat(yT_hi[slot]), ps_yT[:]).then_inc(yT_hi_ready, 1)

            def hi_x(k, slot):
                act.wait_ge(xT_in[slot], 16 * k)
                copy(flat(xT_hi), raw_x(2 * k + slot)).then_inc(xT_hi_ready, 1)

            def hi_wc(k, slot, h):
                act.wait_ge(wc_in[slot][h], 16 * k)
                copy(half(wc_hi, h), raw_half(2 * k + slot, h)).then_inc(wc_hi_ready, 1)

            def copy_z(b, bank):
                act.wait_ge(tzb_done, b + 1)
                copy(z_sb[:], bank[:, ER:TZ]).then_inc(z_copied, 1)

            def exponent(b):
                act.wait_ge(nmax_ready, b + 1)
                nc.scalar.activation(expd[:], nlogit[:], ACT.Exp, bias=nmax[:], scale=-1.0,
                                     accum_out=esum[:]).then_inc(exp_ready, 1)

            def hi_tsT(b):
                act.wait_ge(tsT_done, b + 1)
                copy(tsT_hi[:], ps_tsT[:, 0:S]).then_inc(tsT_hi_ready, 1)

            def store(b, slot):
                act.wait_ge(o_ready, b + 1)
                act.dma_start(out[bass.ds(b, 1)].rearrange("b s d -> (b s) d"), o_sb[slot][:])\
                    .then_inc(stored[slot], 16)

            def step(k, slot):
                b = 2 * k + slot
                hi_tsT(b - 1)
                copy_y(b + 1, ps_y[:])
                hi_x(k + 1, slot)
                for h in range(2):
                    hi_wc(k + 1, slot, h)
                hi_yT(b + 1, 1 - slot)
                copy_z(b, ps_o[slot][:, 0])
                exponent(b)
                store(b - 1, 1 - slot)

            for n, part in enumerate((slice(0, 1), slice(1, C))):
                act.dma_start(xT_raw[:, 0, part, :], xT[0, :, part, :]).then_inc(xT0_in[n], 16)
            act.wait_ge(wc01_in[0][0], 16)
            act.dma_start(xT_raw[:, 1], xT[1]).then_inc(x1_in, 16)

            copy_y(0, ps_y[:])
            hi_yT(0, 0)
            hi_w(0)
            hi_w(1)
            hi_w(2)
            copy_y(1, ps_o[1][:, 0])
            hi_w(3)
            hi_yT(1, 1)
            copy_z(0, ps_o[0][:, 0])
            exponent(0)
            act.wait_ge(b_in, 16)
            nc.scalar.mul(b_hi[:], b_raw[:], LORA_SCALE).then_inc(b_hi_ready, 1)
            with act.Fori(0, PAIRS - 2) as k:
                step(k, 1)
                step(k + 1, 0)
            step(PAIRS - 2, 1)
            hi_tsT(B - 3)
            copy_y(B - 1, ps_y[:])
            hi_yT(B - 1, 1)
            copy_z(B - 2, ps_o[0][:, 0])
            exponent(B - 2)
            copy_z(B - 1, ps_y)
            hi_tsT(B - 2)
            exponent(B - 1)
            hi_tsT(B - 1)

        @block.vector
        def _(dve):
            tt = nc.vector.tensor_tensor

            def lo_w(c):
                dve.wait_ge(w_hi_ready, c + 1)
                tt(w_lo[:, c, :], w_raw[:, c, :], w_hi[:, c, :].bitcast(F32), ALU.subtract)\
                    .then_inc(w_lo_ready, 1)

            def lo_yT(b, slot):
                dve.wait_ge(yT_hi_ready, b + 1)
                tt(flat(yT_lo[slot]), ps_yT[:], flat(yT_hi[slot]).bitcast(F32), ALU.subtract)\
                    .then_inc(yT_lo_ready, 1)

            def lo_wc(b, h):
                dve.wait_ge(wc_hi_ready, halves_split(b, h))
                tt(half(wc_lo, h), raw_half(b, h), half(wc_hi, h).bitcast(F32), ALU.subtract)\
                    .then_inc(wc_lo_ready, 1)

            def negated_logits(b):
                dve.wait_ge(logit_done, b + 1)
                nc.vector.scalar_tensor_tensor(out=nlogit[:], in0=ps_logit[:, 0:E], scalar=-1.0, in1=rbias_bc[:],
                                               op0=ALU.mult, op1=ALU.subtract).then_inc(nlogit_ready, 1)
                dve.wait_ge(nlogit_ready, b + 1)
                nc.vector.tensor_reduce(nmax[:], nlogit[:], mybir.AxisListType.X, ALU.min).then_inc(nmax_ready, 1)

            def scale_t(b, bank):
                dve.wait_ge(exp_ready, b + 1)
                nc.vector.reciprocal(rsum[:], esum[:]).then_inc(rsum_ready, 1)
                dve.wait_ge(rsum_ready, b + 1)
                nc.vector.scalar_tensor_tensor(
                    out=ts[:].rearrange("p (e r) -> p e r", e=E),
                    in0=bank[:, 0:ER].rearrange("p (e r) -> p e r", e=E), scalar=rsum[:, 0:1],
                    in1=expd[:].unsqueeze(2).to_broadcast([P, E, R]), op0=ALU.mult,
                    op1=ALU.mult).then_inc(ts_ready, 1)

            def lo_tsT(b):
                dve.wait_ge(tsT_hi_ready, b + 1)
                tt(tsT_lo[:], ps_tsT[:, 0:S], tsT_hi[:].bitcast(F32), ALU.subtract).then_inc(tsT_lo_ready, 1)

            def add_residual(k, slot):
                b = 2 * k + slot
                dve.wait_ge(o_done, b + 1)
                dve.wait_ge(xb_ready, b + 1)
                if not (isinstance(k, int) and k == 0):
                    dve.wait_ge(stored[slot], 16 * k)
                tt(o_sb[slot][:].rearrange("p (n h) -> p n h", n=2), ps_o[slot][:, :, BASE],
                   x_res[:, bass.ds(b, 1)].rearrange("p b (n h) -> p (b n) h", n=2), ALU.add)\
                    .then_inc(o_ready, 1)

            def step(k, slot):
                b = 2 * k + slot
                lo_tsT(b - 1)
                lo_wc(b + 2, 0)
                lo_wc(b + 2, 1)
                add_residual(k - 1 + slot, 1 - slot)
                negated_logits(b)
                lo_yT(b + 1, 1 - slot)
                scale_t(b, ps_o[slot][:, 0])

            nc.vector.memset(warm[:], 0.0).then_inc(warm_ready, 1)
            lo_yT(0, 0)
            for c in range(C):
                lo_w(c)
            lo_yT(1, 1)
            dve.wait_ge(rbias_in, 16)
            negated_logits(0)
            scale_t(0, ps_o[0][:, 0])
            dve.wait_ge(b_hi_ready, 1)
            nc.vector.scalar_tensor_tensor(out=b_lo[:], in0=b_raw[:], scalar=LORA_SCALE, in1=b_hi[:].bitcast(F32),
                                           op0=ALU.mult, op1=ALU.subtract).then_inc(b_lo_ready, 1)
            step(0, 1)
            with dve.Fori(1, PAIRS - 1) as k:
                for slot in range(2):
                    step(k, slot)
            lo_tsT(B - 3)
            lo_yT(B - 1, 1)
            add_residual(PAIRS - 2, 1)
            negated_logits(B - 2)
            scale_t(B - 2, ps_o[0][:, 0])
            negated_logits(B - 1)
            lo_tsT(B - 2)
            scale_t(B - 1, ps_y)
            lo_tsT(B - 1)
            add_residual(PAIRS - 1, 0)
            dve.wait_ge(xb_ready, B)
            dve.wait_ge(stored[1], 16 * (PAIRS - 1))
            for n in range(2):
                dve.wait_ge(o_done, B + n)
                half_n = slice(n * HALF, (n + 1) * HALF)
                tt(o_sb[1][:, half_n], ps_o[1][:, n, BASE], x_res[:, B - 1, half_n], ALU.add).then_inc(o_ready, 1)

        @block.tensor
        def _(pe):
            mm = nc.tensor.matmul

            def keep_warm(n):
                for _ in range(n):
                    mm(ps_logit[:], warm[:, 0:P], warm[:], start=True, stop=True)

            def y_raw(b, c, bank):
                last = mm(bank, xT_raw[:, b, c, :], wc_raw[:, b, c, :], start=(c == 0), stop=(c == C - 1))
                if c == C - 1:
                    last.then_inc(y_done, 1)

            def y_split(b, c):
                if c == 0:
                    pe.wait_ge(xT_lo_ready, b - SPLIT0 + 1)
                if c % CH == 0:
                    pe.wait_ge(wc_lo_ready, halves_split(b, c // CH))
                mm(ps_y[:], xT_hi[:, c, :], wc_hi[:, c, :], start=(c == 0), stop=False)
                mm(ps_y[:], xT_hi[:, c, :], wc_lo[:, c, :], start=False, stop=False)
                last = mm(ps_y[:], xT_lo[:, c, :], wc_hi[:, c, :], start=False, stop=(c == C - 1))
                if c == C - 1:
                    last.then_inc(y_done, 1)

            def transpose_y(b):
                pe.wait_ge(y_copied, b + 1)
                for c in range(C):
                    last = nc.tensor.transpose(ps_yT[:, c * S:(c + 1) * S], y_sb[:, c * P:(c + 1) * P], ident[:])
                last.then_inc(yT_done, 1)

            FIRST = (slice(0, TZ + HALF), 0, slice(0, TZ + HALF))
            SECOND = (slice(TZ + HALF, TZ + D), 1, BASE)

            def products(b, slot, c, parts, banks):
                for stat, mov, n in ((yT_hi, w_hi, 0), (yT_hi, w_lo, 1), (yT_lo, w_hi, 2)):
                    for cols, bank, to in parts:
                        last = mm(banks[:, bank, to], stat[slot][:, c, :], mov[:, c, cols],
                                  start=(c == 0 and n == 0), stop=(c == C - 1 and n == 2))
                return last

            def wait_yT(b):
                pe.wait_ge(yT_hi_ready, b + 1)
                pe.wait_ge(yT_lo_ready, b + 1)

            def logits(b):
                pe.wait_ge(z_copied, b + 1)
                mm(ps_logit[:, 0:E], mean_w[:], z_sb[:], start=True, stop=True).then_inc(logit_done, 1)

            def transpose_t(b):
                pe.wait_ge(ts_ready, b + 1)
                nc.tensor.transpose(ps_tsT[:, 0:S], ts[:], ident[:]).then_inc(tsT_done, 1)

            def lora_half(b, slot, n):
                pe.wait_ge(tsT_hi_ready, b + 1)
                pe.wait_ge(tsT_lo_ready, b + 1)
                for stat, mov in ((tsT_hi, b_hi), (tsT_hi, b_lo), (tsT_lo, b_hi)):
                    last = mm(ps_o[slot][:, n, BASE], stat[:], mov[:, n * HALF:(n + 1) * HALF], start=False,
                              stop=False, skip_group_check=True)
                return last

            def lora(b, slot):
                lora_half(b, slot, 0)
                lora_half(b, slot, 1).then_inc(o_done, 1)

            def step(k, slot):
                b = 2 * k + slot
                wait_yT(b)
                if not (isinstance(k, int) and k == 0):
                    pe.wait_ge(o_ready, b - 1)
                products(b, slot, 0, (FIRST, SECOND), ps_o[slot])
                products(b, slot, 1, (FIRST, SECOND), ps_o[slot])
                transpose_y(b + 1)
                lora(b - 1, 1 - slot)
                products(b, slot, 2, (FIRST, SECOND), ps_o[slot])
                products(b, slot, 3, (FIRST, SECOND), ps_o[slot]).then_inc(tzb_done, 1)
                y_split(b + 2, 0)
                logits(b)
                for c in range(1, C):
                    y_split(b + 2, c)
                transpose_t(b)

            pe.wait_ge(warm_ready, 1)
            keep_warm(WARM_UPS)
            for c in range(C):
                if c < 2:
                    pe.wait_ge(xT0_in[c], 16)
                pe.wait_ge(wc01_in[0][c], 16)
                y_raw(0, c, ps_y[:])
            pe.wait_ge(x1_in, 16)
            for c in range(C):
                pe.wait_ge(wc01_in[1][c], 16)
                y_raw(1, c, ps_o[1][:, 0])
                if c == 0:
                    pe.wait_ge(ident_ready, 1)
                    transpose_y(0)
            wait_yT(0)
            for c in range(C):
                pe.wait_ge(w_lo_ready, c + 1)
                last = products(0, 0, c, (FIRST, SECOND), ps_o[0])
                if c == 1:
                    transpose_y(1)
            last.then_inc(tzb_done, 1)
            pe.wait_ge(xT_in[0], 16)
            for c in range(C):
                if c % CH == 0:
                    pe.wait_ge(wc_in[0][c // CH], 16)
                y_raw(2, c, ps_y[:])
                if c == 0:
                    pe.wait_ge(mean_ready, 1)
                    logits(0)
            transpose_t(0)
            pe.wait_ge(b_hi_ready, 1)
            pe.wait_ge(b_lo_ready, 1)

            step(0, 1)
            with pe.Fori(1, PAIRS - 1) as k:
                for slot in range(2):
                    step(k, slot)

            b, slot = B - 2, 0
            wait_yT(b)
            pe.wait_ge(o_ready, b - 1)
            for c in range(C):
                if c == CH:
                    transpose_y(b + 1)
                    lora(b - 1, 1)
                last = products(b, slot, c, (FIRST,), ps_o[slot])
            last.then_inc(tzb_done, 1)

            wait_yT(B - 1)
            for c in range(C):
                last = products(B - 1, 1, c, ((slice(0, TZ), 0, slice(0, TZ)),), ps_y[:].unsqueeze(1))
                if c == CH - 1:
                    logits(B - 2)
            last.then_inc(tzb_done, 1)
            for c in range(C):
                products(B - 2, 0, c, (SECOND,), ps_o[0])
                if c == CH:
                    logits(B - 1)
            transpose_t(B - 2)
            pe.wait_ge(o_ready, B - 2)
            for c in range(C):
                if c == C - 1:
                    lora(B - 2, 0)
                    transpose_t(B - 1)
                products(B - 1, 1, c, ((slice(TZ, TZ + HALF), 0, BASE),), ps_o[1])
            products(B - 1, 1, 0, (SECOND,), ps_o[1])
            products(B - 1, 1, 1, (SECOND,), ps_o[1])
            lora_half(B - 1, 1, 0).then_inc(o_done, 1)
            products(B - 1, 1, 2, (SECOND,), ps_o[1])
            products(B - 1, 1, 3, (SECOND,), ps_o[1])
            lora_half(B - 1, 1, 1).then_inc(o_done, 1)


def kernel(x, itok_B_1_14, L0_cond_weight, L0_ffn_W, L0_ffn_b, L0_ffn_A, L0_ffn_B, L0_ffn_router_W,
           L0_ffn_router_b):
    import numpy as np
    import concourse.bacc as bacc
    from concourse.bass_utils import run_bass_kernel_spmd

    x, wc, w, bias, a, b, rw, rb = (np.asarray(v) for v in (
        x, L0_cond_weight, L0_ffn_W, L0_ffn_b, L0_ffn_A, L0_ffn_B, L0_ffn_router_W, L0_ffn_router_b))
    nb, s, d = x.shape
    c = d // P
    e, r, _ = a.shape

    def contraction_first(m):
        m = np.moveaxis(m.reshape(*m.shape[:-1], c, P), (-1, -2), (-3, -2))
        return np.ascontiguousarray(m)

    arrays = {
        "x": np.ascontiguousarray(x),
        "xT": contraction_first(x),
        "ids": np.ascontiguousarray(np.asarray(itok_B_1_14).reshape(1, nb)),
        "wcT": contraction_first(wc),
        "azwT": contraction_first(np.concatenate([a.reshape(e * r, d), rw, w])),
        "bT": np.ascontiguousarray(b.transpose(0, 2, 1).reshape(e * r, d)),
        "bias": np.ascontiguousarray(bias.reshape(1, d)),
        "rbias": np.ascontiguousarray(rb.reshape(1, e)),
    }
    nc = bacc.Bacc("TRN2", target_bir_lowering=False, num_devices=1)
    args = [nc.dram_tensor(f"in_{n}_dram", v.shape, mybir.dt.from_np(v.dtype), kind="ExternalInput").ap()
            for n, v in arrays.items()]
    out = nc.dram_tensor("out_0_dram", x.shape, F32, kind="ExternalOutput").ap()
    adapter_lora_kernel(nc, *args, out)
    got = run_bass_kernel_spmd(nc, [{f"in_{n}_dram": v for n, v in arrays.items()}], core_ids=[0])
    return got.results[0]["out_0_dram"]
```
